# Optimizing a Trainium2 kernel written in Bass

```python
import numpy as np
import jax
import jax.numpy as jnp

def _softmax(x, axis=-1):
    return jax.nn.softmax(x, axis=axis)

def _gelu(x):
    return jax.nn.gelu(x, approximate=True)

def _silu(x):
    return jax.nn.silu(x)

def _sigmoid(x):
    return jax.nn.sigmoid(x)

def _layernorm(x, axis=-1, eps=1e-05):
    m = jnp.mean(x, axis=axis, keepdims=True)
    v = jnp.var(x, axis=axis, keepdims=True)
    return (x - m) / jnp.sqrt(v + eps)

def _scatter_add(tgt, idx, src, axis=0):
    return tgt.at[idx].add(src)

def _segment_sum(src, seg, n):
    return jax.ops.segment_sum(src, seg, n)
kernel_name = 'mk_rec_standalone_d1_rec_r8_dde62c'

def setup_inputs(seed: int=0):
    np.random.seed(seed)
    _w = jnp.asarray

    def _rec_inputs():
        import jax
        import jax.numpy as jnp
        _rk = jax.random.key(seed)
        r_target_item = -9.80646e-05 + 1.00041 * jax.random.normal(jax.random.fold_in(_rk, 1), (2048, 128), jnp.float32)
        r_history_sequence = -9.97791e-05 + 0.999858 * jax.random.normal(jax.random.fold_in(_rk, 2), (2048, 200, 128), jnp.float32)
        r_mask = jax.random.randint(jax.random.fold_in(_rk, 3), (2048, 200), 0, 2, jnp.int32)
        return (r_target_item, r_history_sequence, r_mask)
    r_target_item, r_history_sequence, r_mask = _rec_inputs()

    def _L0_rec_setup():
        import jax, jax.numpy as jnp
        import numpy as np
        B, S, D = (512, 200, 128)
        A, H = (128, 4)
        HD = A // H
        SCALE = HD ** 0.5
        NEG = -1000000000.0
        key = jax.random.key(seed)
        ks = jax.random.split(key, 7)
        return {'target_item': jax.random.normal(ks[0], (B, D), dtype=jnp.float32), 'history_sequence': jax.random.normal(ks[1], (B, S, D), dtype=jnp.float32), 'mask': jax.random.randint(ks[2], (B, S), 0, 2, dtype=jnp.int32), 'W_q': jax.random.normal(ks[3], (D, A), dtype=jnp.float32) / np.sqrt(D), 'W_k': jax.random.normal(ks[4], (D, A), dtype=jnp.float32) / np.sqrt(D), 'W_v': jax.random.normal(ks[5], (D, A), dtype=jnp.float32) / np.sqrt(D), 'W_o': jax.random.normal(ks[6], (A, D), dtype=jnp.float32) / np.sqrt(A)}
    _L0_rec_all = _L0_rec_setup()
    _L0_rec_in = {k: v for k, v in _L0_rec_all.items() if k in ('W_q', 'W_k', 'W_v', 'W_o')}
    del _L0_rec_all
    return {'r_target_item': r_target_item, 'r_history_sequence': r_history_sequence, 'r_mask': r_mask, 'L0_rec_W_q': _L0_rec_in['W_q'], 'L0_rec_W_k': _L0_rec_in['W_k'], 'L0_rec_W_v': _L0_rec_in['W_v'], 'L0_rec_W_o': _L0_rec_in['W_o']}

def reference(r_target_item, r_history_sequence, r_mask, L0_rec_W_q, L0_rec_W_k, L0_rec_W_v, L0_rec_W_o):
    import jax
    import jax.numpy as jnp

    def _L0_rec_ref(target_item, history_sequence, mask, W_q, W_k, W_v, W_o):
        import jax, jax.numpy as jnp
        import numpy as np
        B, S, D = (512, 200, 128)
        A, H = (128, 4)
        HD = A // H
        SCALE = HD ** 0.5
        NEG = -1000000000.0
        b = target_item.shape[0]
        q = (target_item @ W_q).reshape(b, H, HD)
        k = (history_sequence @ W_k).reshape(b, S, H, HD)
        v = (history_sequence @ W_v).reshape(b, S, H, HD)
        scores = jnp.einsum('bhd,bshd->bhs', q, k) / SCALE
        scores = jnp.where(mask[:, None, :] == 0, NEG, scores)
        attn = jax.nn.softmax(scores, axis=-1)
        out = jnp.einsum('bhs,bshd->bhd', attn, v).reshape(b, A)
        return out @ W_o
    y = _L0_rec_ref(r_target_item, r_history_sequence, r_mask, L0_rec_W_q, L0_rec_W_k, L0_rec_W_v, L0_rec_W_o)
    return y

_drawn_inputs = setup_inputs


def setup_inputs(seed=0):
    import zlib

    import numpy as np

    out = dict(_drawn_inputs(seed))
    spreads = {}
    factors = {}
    for name, (base, spread) in spreads.items():
        noise = np.random.default_rng([zlib.crc32(name.encode()), seed]).standard_normal(out[name].shape)
        drawn = base * np.exp(spread * noise) if base else spread * noise
        out[name] = jnp.asarray(drawn.astype(out[name].dtype))
    for name, factor in factors.items():
        out[name] = (out[name] * factor).astype(out[name].dtype)
    return out
```

```python
from contextlib import ExitStack

import concourse.bass as bass
from concourse import mybir

ALU = mybir.AluOpType
ACT = mybir.ActivationFunctionType
F32 = mybir.dt.float32
I32 = mybir.dt.int32


def target_attention(nc, target, history, mask, w_q, w_k, w_v, w_o, out):
    B, S, D = history.shape
    P = 128
    H = 4
    HD = D // H
    HALF = S // 2
    SPLIT = 96
    TILES = 4
    PAIR = 2
    QUAD = 4
    STEP = TILES * PAIR
    STEPS = 4
    GROUPS = 4
    GROUP = STEP * STEPS
    SLOTS = STEPS * GROUPS
    ROUND = GROUP * GROUPS
    ROUNDS = B // ROUND
    BANKS = STEP // 2
    LAG_S = 1
    LAG_C = 6
    TAIL = 7
    NEG = 1e9
    INV_SCALE = float(HD) ** -0.5
    assert D == P and H * GROUP == P and HALF <= P and B % ROUND == 0

    history_v = history.rearrange("b (p t) d -> p b (t d)", t=2)

    with ExitStack() as ctx:
        def sb(name, shape, dt=F32):
            return ctx.enter_context(nc.sbuf_tensor(name, shape, dt))

        def ps(name, shape):
            return ctx.enter_context(nc.psum_tensor(name, shape, F32))

        def sem(name):
            return ctx.enter_context(nc.semaphore(name))

        hist = sb("hist", [P, SLOTS, STEP, 2, D])
        hist_t = [sb(f"hist_t{i}", [P, STEP, S]) for i in range(2)]
        u_pad = [sb(f"u_pad{i}", [P, STEPS, TILES, 32]) for i in range(2)]
        p_pad = [sb(f"p_pad{i}", [P, 2, STEPS // 2, TILES, 32]) for i in range(2)]
        x_sb = sb("x_sb", [P, D])
        x_t = sb("x_t", [P, ROUND])
        u_sb = sb("u_sb", [P, ROUND, H])
        pair_sel = sb("pair_sel", [P, PAIR])
        quad_sel = sb("quad_sel", [P, QUAD])
        sel_sum = sb("sel_sum", [P, PAIR])
        mask_sb = [sb(f"mask{g}", [P, S], I32) for g in range(GROUPS)]
        keep = [sb(f"keep{i}", [P, S]) for i in range(2)]
        fill = [sb(f"fill{i}", [P, S]) for i in range(2)]
        half_score = sb("half_score", [P, S])
        full_score = sb("full_score", [P, S])
        kept = sb("kept", [P, S])
        neg_score = sb("neg_score", [P, S])
        neg_max = sb("neg_max", [P, 1])
        probs = sb("probs", [P, S])
        row_sum = sb("row_sum", [P, 1])
        inv_sum = sb("inv_sum", [P, 1])
        quad_inv = sb("quad_inv", [P, QUAD])
        ctx_part = [sb(f"ctx_part{i}", [P, D]) for i in range(QUAD - 1)]
        ctx_sb = sb("ctx_sb", [P, D])
        ctx_t = sb("ctx_t", [P, H, ROUND])
        out_sb = sb("out_sb", [ROUND, D])
        w_in = sb("w_in", [P, 4, P])
        w_t = sb("w_t", [P, 3, P])
        w_head = sb("w_head", [P, H, 2, P])
        ident = sb("ident", [P, P])

        ps_t = [ps(f"ps_t{q}", [P, 512]) for q in range(BANKS)]
        ps_s = ps("ps_s", [P, 512])
        ps_c = ps("ps_c", [P, 512])
        ps_p = ps("ps_p", [P, 512])
        ps_y = ps("ps_y", [P, 512])

        w_loaded = sem("w_loaded")
        x_loaded = sem("x_loaded")
        hist_loaded = [sem(f"hist_loaded{s}") for s in range(SLOTS)]
        mask_loaded = [sem(f"mask_loaded{g}") for g in range(GROUPS)]
        out_stored = sem("out_stored")
        zeroed = sem("zeroed")
        ident_ready = sem("ident_ready")
        u_pad_zero = sem("u_pad_zero")
        p_pad_zero = sem("p_pad_zero")
        w_t_done = sem("w_t_done")
        w_t_copied = sem("w_t_copied")
        w_head_done = sem("w_head_done")
        w_head_act = sem("w_head_act")
        w_head_dve = sem("w_head_dve")
        x_t_done = sem("x_t_done")
        x_t_copied = sem("x_t_copied")
        u_done = sem("u_done")
        u_copied = sem("u_copied")
        banks_done = sem("banks_done")
        even_copied = sem("even_copied")
        odd_copied = sem("odd_copied")
        u_pad_ready = sem("u_pad_ready")
        fill_ready = sem("fill_ready")
        mask_ready = sem("mask_ready")
        scores_done = sem("scores_done")
        sel_ready = sem("sel_ready")
        half_ready = sem("half_ready")
        scores_read = sem("scores_read")
        kept_ready = sem("kept_ready")
        masked = sem("masked")
        max_ready = sem("max_ready")
        exp_done = sem("exp_done")
        inv_ready = sem("inv_ready")
        probs_t_done = sem("probs_t_done")
        p_pad_ready = sem("p_pad_ready")
        ctx_done = sem("ctx_done")
        quad_inv_ready = sem("quad_inv_ready")
        ctx_part_ready = sem("ctx_part_ready")
        ctx_copied = sem("ctx_copied")
        ctx_t_done = sem("ctx_t_done")
        ctx_t_copied = sem("ctx_t_copied")
        out_done = sem("out_done")
        out_copied = sem("out_copied")

        block = ctx.enter_context(nc.Block())

        def wait(eng, semaphore, rnd, per_round, offset):
            count = rnd * per_round + offset
            if isinstance(rnd, int):
                if count > 0:
                    eng.wait_ge(semaphore, count)
            else:
                assert per_round + offset > 0
                eng.wait_ge(semaphore, count)

        def rounds(eng, one_round):
            one_round(0, range(SLOTS), True, False)
            with eng.Fori(1, ROUNDS) as rnd:
                one_round(rnd, range(SLOTS), False, False)
            one_round(ROUNDS, range(TAIL), False, True)

        def pad_columns(pad, shares, width):
            return bass.AP(pad.tensor, pad.offset,
                           [list(pad.ap[0]), [32 * TILES + width, shares], [32, TILES], [1, width]])

        @block.sync
        def _(sp):
            for n, w in enumerate((w_q, w_k, w_v, w_o)):
                sp.dma_start(w_in[:, n, :], w).then_inc(w_loaded, 16)

            def one_round(rnd, slots, first, tail):
                if tail:
                    return
                wait(sp, x_t_done, rnd, 1, 0)
                sp.dma_start(x_sb[:, :], target[bass.ds(rnd * ROUND, ROUND), :]).then_inc(x_loaded, 16)
                for s in slots:
                    gr, k = divmod(s, STEPS)
                    wait(sp, ctx_done, rnd, SLOTS // 2, s // 2 + 1 - SLOTS // 2)
                    for a, b in ((0, SPLIT), (SPLIT, HALF)):
                        sp.dma_start(
                            hist[a:b, s].rearrange("p b t d -> p b (t d)"),
                            history_v[a:b, bass.ds(rnd * ROUND + s * STEP, STEP), :],
                        ).then_inc(hist_loaded[s], 16)
                    if k == 0:
                        wait(sp, mask_ready, rnd, GROUPS, gr + 1 - GROUPS)
                        rows = mask[bass.ds(rnd * ROUND + gr * GROUP, GROUP), :]
                        sp.dma_start(mask_sb[gr][:, :],
                                     rows.unsqueeze(1).broadcast_to([GROUP, H, S])).then_inc(mask_loaded[gr], 16)

            rounds(sp, one_round)
            sp.wait_ge(out_stored, 16 * ROUNDS)

        @block.gpsimd
        def _(pool):
            pool.memset(ident[:, :], 0.0).then_inc(zeroed, 1)
            pool.wait_ge(zeroed, 1)
            pool.affine_select(out=ident[:, :], in_=ident[:, :], compare_op=ALU.not_equal, fill=1.0,
                               base=0, pattern=[[-1, P]], channel_multiplier=1).then_inc(ident_ready, 1)
            for pad in u_pad:
                pool.memset(pad[:, :, :, :], 0.0).then_inc(u_pad_zero, 1)
            def one_round(rnd, slots, first, tail):
                for s in slots:
                    if (s == 2 * STEPS + 1 or (tail and s == TAIL - 1)) and not first:
                        wait(pool, out_copied, rnd, 1, 0)
                        pool.dma_start(out[bass.ds((rnd - 1) * ROUND, ROUND), :],
                                       out_sb[:, :]).then_inc(out_stored, 16)

            rounds(pool, one_round)

        @block.tensor
        def _(pe):
            pe.wait_ge(ident_ready, 1)
            pe.wait_ge(w_loaded, 64)
            for n in range(3):
                mm = pe.transpose(ps_p[:, n * P:(n + 1) * P], w_in[:, n, :], ident[:, :])
            mm.then_inc(w_t_done, 1)
            pe.wait_ge(w_t_copied, 1)
            for h in range(H):
                rows = slice(h * HD, (h + 1) * HD)
                pe.matmul(ps_t[h][:, 0:P], w_t[rows, 0, :], w_t[rows, 1, :], start=True, stop=True)
                pe.matmul(ps_t[h][:, P:2 * P], w_t[rows, 2, :], w_in[rows, 3, :],
                          start=True, stop=True).then_inc(w_head_done, 1)

            def one_round(rnd, slots, first, tail):
                for s in slots:
                    gr, k = divmod(s, STEPS)
                    if s == 0 and not tail:
                        wait(pe, x_loaded, rnd, 16, 16)
                        wait(pe, ctx_t_copied, rnd, PAIR * GROUPS, -2 * PAIR)
                        pe.transpose(ps_y[:, 0:ROUND], x_sb[:, :], ident[:, :]).then_inc(x_t_done, 1)
                    if not tail:
                        wait(pe, hist_loaded[s], rnd, 32, 32)
                        for q in range(BANKS):
                            if first and s == 0:
                                pe.wait_ge(w_head_act if q % 2 == 0 else w_head_dve, 2)
                            wait(pe, even_copied if q % 2 == 0 else odd_copied, rnd, 2 * SLOTS,
                                 2 * (s - 1) + q // 2 + 1)
                            for j in (2 * q, 2 * q + 1):
                                for t in range(2):
                                    at = (j % 2) * S + t * HALF
                                    mm = pe.transpose(ps_t[q][:, at:at + HALF], hist[0:HALF, s, j, t, :],
                                                      ident[0:HALF, 0:HALF])
                            mm.then_inc(banks_done, 1)
                    if s == 0 and not tail:
                        wait(pe, x_t_copied, rnd, 1, 1)
                        wait(pe, p_pad_ready, rnd, 2 * GROUPS, -2)
                        for h in range(H):
                            mm = pe.matmul(ps_p[:, h * ROUND:(h + 1) * ROUND], w_head[:, h, 0, :],
                                           x_t[:, :], start=True, stop=True)
                        mm.then_inc(u_done, 1)
                    if not (first and s < LAG_S) and not (tail and s >= LAG_S):
                        m = (s - LAG_S) % SLOTS
                        mg, mk = divmod(m, STEPS)
                        wait(pe, even_copied, rnd, 2 * SLOTS, 2 * (s - LAG_S + 1))
                        wait(pe, odd_copied, rnd, 2 * SLOTS, 2 * (s - LAG_S + 1))
                        if mk == 0:
                            wait(pe, u_pad_ready, rnd, GROUPS, mg + 1)
                            wait(pe, scores_read, rnd, GROUPS, mg)
                        for g in range(TILES):
                            mm = pe.matmul(ps_s[32 * g:32 * g + 32, 0:PAIR * S], u_pad[mg % 2][:, mk, g, :],
                                           hist_t[m % 2][:, PAIR * g:PAIR * (g + 1), :],
                                           start=(mk == 0), stop=(mk == STEPS - 1))
                        mm.then_inc(scores_done, 1)
                    if k == 1 and not (first and gr == 0) and not (tail and gr > 0):
                        wait(pe, exp_done, rnd, GROUPS, gr)
                        if gr == 0 and not tail:
                            wait(pe, u_copied, rnd, 1, 1)
                        else:
                            wait(pe, p_pad_ready, rnd, 2 * GROUPS, 2 * (gr - 1))
                        for t in range(2):
                            mm = pe.transpose(ps_p[0:HALF, t * P:(t + 1) * P],
                                              probs[:, t * HALF:(t + 1) * HALF], ident[:, :])
                        mm.then_inc(probs_t_done, 1)
                    if k == 1 and not (first and gr < 2):
                        wait(pe, ctx_copied, rnd, GROUPS, gr - 1)
                        if gr == 0 and not tail:
                            wait(pe, x_t_copied, rnd, 1, 1)
                        elif gr == 2:
                            wait(pe, out_copied, rnd, 1, 0)
                        else:
                            wait(pe, ctx_t_copied, rnd, PAIR * GROUPS, PAIR * (gr - 2))
                        pe.transpose(ps_y[:, P:2 * P], ctx_sb[:, :], ident[:, :]).then_inc(ctx_t_done, 1)
                    if s == STEPS + 2 and not first:
                        wait(pe, ctx_t_copied, rnd, PAIR * GROUPS, 0)
                        for h in range(H):
                            mm = pe.matmul(ps_y[:, 2 * P:3 * P], ctx_t[:, h, :], w_head[:, h, 1, :],
                                           start=(h == 0), stop=(h == H - 1))
                        mm.then_inc(out_done, 1)
                    if s % 2 == 0 and not (first and s < LAG_C) and not (tail and s >= LAG_C):
                        m = (s - LAG_C) % SLOTS
                        mg, mk = divmod(m, STEPS)
                        behind = GROUPS if s < LAG_C else 0
                        if mk == 0:
                            wait(pe, p_pad_ready, rnd, 2 * GROUPS, 2 * (mg + 1 - behind))
                            wait(pe, ctx_copied, rnd, GROUPS, mg - behind)
                        for t in range(2):
                            for g in range(TILES):
                                mm = pe.matmul(ps_c[32 * g:32 * g + 32, :],
                                               p_pad[mg % 2][0:HALF, t, mk // 2, g, :],
                                               hist[0:HALF, m:m + 2, PAIR * g:PAIR * (g + 1), t, :],
                                               start=(mk == 0 and t == 0),
                                               stop=(mk == STEPS - 2 and t == 1))
                        mm.then_inc(ctx_done, 1)

            rounds(pe, one_round)

        @block.scalar
        def _(act):
            act.wait_ge(w_t_done, 1)
            act.copy(w_t[:, :, :], ps_p[:, 0:3 * P].rearrange("p (n c) -> p n c", n=3)).then_inc(w_t_copied, 1)
            for h in (0, 2):
                act.wait_ge(w_head_done, h + 1)
                act.copy(w_head[:, h, :, :],
                         ps_t[h][:, 0:2 * P].rearrange("p (n c) -> p n c", n=2)).then_inc(w_head_act, 1)

            def one_round(rnd, slots, first, tail):
                for s in slots:
                    gr, k = divmod(s, STEPS)
                    if s == 0 and not tail:
                        wait(act, x_t_done, rnd, 1, 1)
                        wait(act, u_done, rnd, 1, 0)
                        act.copy(x_t[:, :], ps_y[:, 0:ROUND]).then_inc(x_t_copied, 1)
                    if not tail:
                        for q in (0, 2):
                            wait(act, banks_done, rnd, BANKS * SLOTS, BANKS * s + q + 1)
                            wait(act, scores_done, rnd, SLOTS, s - 1)
                            act.copy(hist_t[s % 2][:, 2 * q:2 * q + 2, :],
                                     ps_t[q][:, 0:2 * S].rearrange("p (j c) -> p j c", j=2)
                                     ).then_inc(even_copied, 1)
                    if s == 0 and not tail:
                        wait(act, u_done, rnd, 1, 1)
                        wait(act, u_pad_ready, rnd, GROUPS, 0)
                        act.copy(u_sb[:, :, :],
                                 ps_p[:, :].rearrange("p (h b) -> p b h", h=H)).then_inc(u_copied, 1)
                    if k == 0 and not (first and gr == 0) and not (tail and gr > 0):
                        wait(act, max_ready, rnd, GROUPS, gr)
                        wait(act, probs_t_done, rnd, GROUPS, gr - 1)
                        wait(act, inv_ready, rnd, GROUPS, gr - 1)
                        act.activation(probs[:, :], neg_score[:, :], ACT.Exp, bias=neg_max[:, 0:1],
                                       scale=-1.0, accum_out=row_sum[:, 0:1]).then_inc(exp_done, 1)
                    if k == 1 and not (first and gr < 2):
                        g_of = (gr - 2) % GROUPS
                        wait(act, ctx_t_done, rnd, GROUPS, gr - 1)
                        if g_of == 0:
                            wait(act, out_done, rnd, 1, 0)
                        of_group = ctx_t[:, :, g_of * GROUP:(g_of + 1) * GROUP]
                        of_group = of_group.rearrange("p h (k g e) -> p e h g k", g=TILES, e=PAIR)
                        turned = ps_y[:, P:2 * P].rearrange("p (g k e h) -> p e h g k", g=TILES, e=PAIR, h=H)
                        for e in range(PAIR):
                            act.copy(of_group[:, e], turned[:, e]).then_inc(ctx_t_copied, 1)

            rounds(act, one_round)

        @block.vector
        def _(dve):
            for pad in p_pad:
                dve.memset(pad[:, :, :, :, :], 0.0).then_inc(p_pad_zero, 1)
            dve.wait_ge(p_pad_zero, 2)
            dve.wait_ge(u_pad_zero, 2)
            dve.wait_ge(ident_ready, 1)
            dve.tensor_reduce(quad_sel[:, :], ident[:, :].rearrange("p (a c h) -> p c a h", c=QUAD, h=H),
                              mybir.AxisListType.XY, ALU.add).then_inc(sel_ready, 1)
            dve.tensor_reduce(sel_sum[:, :], ident[:, :].rearrange("p (a e h) -> p e a h", e=PAIR, h=H),
                              mybir.AxisListType.XY, ALU.add).then_inc(sel_ready, 1)
            dve.wait_ge(sel_ready, 2)
            dve.tensor_scalar(pair_sel[:, :], sel_sum[:, :], -INV_SCALE, None, ALU.mult).then_inc(sel_ready, 1)
            dve.wait_ge(sel_ready, 3)
            for h in (1, 3):
                dve.wait_ge(w_head_done, h + 1)
                dve.tensor_copy(w_head[:, h, :, :],
                                ps_t[h][:, 0:2 * P].rearrange("p (n c) -> p n c", n=2)
                                ).then_inc(w_head_dve, 1)

            def one_round(rnd, slots, first, tail):
                for s in slots:
                    gr, k = divmod(s, STEPS)
                    if not tail:
                        for q in (1, 3):
                            wait(dve, banks_done, rnd, BANKS * SLOTS, BANKS * s + q + 1)
                            wait(dve, scores_done, rnd, SLOTS, s - 1)
                            dve.tensor_copy(hist_t[s % 2][:, 2 * q:2 * q + 2, :],
                                            ps_t[q][:, 0:2 * S].rearrange("p (j c) -> p j c", j=2)
                                            ).then_inc(odd_copied, 1)
                    if k == 0 and not (first and gr == 0) and not (tail and gr > 0):
                        par = (gr - 1) % 2
                        wait(dve, scores_done, rnd, SLOTS, STEPS * gr)
                        wait(dve, mask_ready, rnd, GROUPS, gr)
                        wait(dve, scores_read, rnd, GROUPS, gr - 1)
                        dve.tensor_scalar(half_score[:, :], ps_s[:, 0:S], pair_sel[:, 0:1], None,
                                          ALU.mult).then_inc(half_ready, 1)
                        wait(dve, kept_ready, rnd, GROUPS, gr - 1)
                        wait(dve, half_ready, rnd, GROUPS, gr)
                        dve.scalar_tensor_tensor(full_score[:, :], ps_s[:, S:2 * S], pair_sel[:, 1:2],
                                                 half_score[:, :], ALU.mult,
                                                 ALU.add).then_inc(scores_read, 1)
                        wait(dve, masked, rnd, GROUPS, gr - 1)
                        wait(dve, scores_read, rnd, GROUPS, gr)
                        dve.tensor_tensor(kept[:, :], full_score[:, :], keep[par][:, :],
                                          ALU.mult).then_inc(kept_ready, 1)
                        wait(dve, exp_done, rnd, GROUPS, gr - 1)
                        wait(dve, kept_ready, rnd, GROUPS, gr)
                        dve.tensor_tensor(neg_score[:, :], kept[:, :], fill[par][:, :],
                                          ALU.add).then_inc(masked, 1)
                        wait(dve, masked, rnd, GROUPS, gr)
                        dve.tensor_reduce(neg_max[:, 0:1], neg_score[:, :], mybir.AxisListType.X,
                                          ALU.min).then_inc(max_ready, 1)
                    if k == 0 and not (first and gr < 2):
                        wait(dve, ctx_part_ready, rnd, GROUPS * (QUAD - 1), (QUAD - 1) * (gr - 2))
                        wait(dve, ctx_copied, rnd, GROUPS, gr - 2)
                        wait(dve, inv_ready, rnd, GROUPS, gr - 1)
                        dve.tensor_scalar(quad_inv[:, :], quad_sel[:, :], inv_sum[:, 0:1], None,
                                          ALU.mult).then_inc(quad_inv_ready, 1)
                        wait(dve, quad_inv_ready, rnd, GROUPS, gr - 1)
                        wait(dve, ctx_done, rnd, SLOTS // 2, STEPS // 2 * (gr - 1))
                        dve.tensor_scalar(ctx_part[0][:, :], ps_c[:, 0:D], quad_inv[:, 0:1], None,
                                          ALU.mult).then_inc(ctx_part_ready, 1)
                        for c in range(1, QUAD):
                            last = c == QUAD - 1
                            if last:
                                wait(dve, ctx_t_done, rnd, GROUPS, gr - 2)
                            wait(dve, ctx_part_ready, rnd, GROUPS * (QUAD - 1), (QUAD - 1) * (gr - 2) + c)
                            dve.scalar_tensor_tensor(
                                (ctx_sb if last else ctx_part[c])[:, :], ps_c[:, c * D:(c + 1) * D],
                                quad_inv[:, c:c + 1], ctx_part[c - 1][:, :], ALU.mult, ALU.add,
                            ).then_inc(ctx_copied if last else ctx_part_ready, 1)
                    if k == 1 and not (first and gr == 0) and not (tail and gr > 0):
                        par = (gr - 1) % 2
                        wait(dve, exp_done, rnd, GROUPS, gr)
                        wait(dve, quad_inv_ready, rnd, GROUPS, gr - 1)
                        dve.reciprocal(inv_sum[:, :], row_sum[:, :]).then_inc(inv_ready, 1)
                        wait(dve, ctx_done, rnd, SLOTS // 2, STEPS // 2 * (gr - 2))
                        wait(dve, probs_t_done, rnd, GROUPS, gr)
                        for t in range(2):
                            dve.tensor_copy(
                                pad_columns(p_pad[par][0:HALF, t], STEPS // 2, 16),
                                ps_p[0:HALF, t * P:(t + 1) * P].rearrange("p (g n c) -> p n g c", g=TILES, c=16),
                            ).then_inc(p_pad_ready, 1)
                    if not tail and (s == 0 or (k == 2 and gr < GROUPS - 1)):
                        ug = 0 if s == 0 else gr + 1
                        wait(dve, scores_done, rnd, SLOTS, STEPS * (ug - 1))
                        if s == 0:
                            wait(dve, u_copied, rnd, 1, 1)
                        dve.tensor_copy(
                            pad_columns(u_pad[ug % 2][:, :, :, :], STEPS, 8),
                            u_sb[:, ug * GROUP:(ug + 1) * GROUP, :].rearrange(
                                "p (k g e) h -> p k g (e h)", g=TILES, e=PAIR),
                        ).then_inc(u_pad_ready, 1)
                    if k == 3 and not tail:
                        wait(dve, max_ready, rnd, GROUPS, gr - 1)
                        wait(dve, mask_loaded[gr], rnd, 16, 16)
                        dve.tensor_scalar(fill[gr % 2][:, :].rearrange("p (t q) -> p t q", t=2),
                                          mask_sb[gr][:, :].rearrange("p (q t) -> p t q", t=2),
                                          0.0, NEG, ALU.is_equal, ALU.mult).then_inc(fill_ready, 1)
                        wait(dve, fill_ready, rnd, GROUPS, gr + 1)
                        dve.tensor_scalar(keep[gr % 2][:, :], fill[gr % 2][:, :], 0.5, None,
                                          ALU.is_lt).then_inc(mask_ready, 1)
                    if s == SLOTS - 1 and not first:
                        wait(dve, out_stored, rnd, 16, 0)
                    if s == STEPS + 2 and not first:
                        wait(dve, out_done, rnd, 1, 0)
                        dve.tensor_copy(out_sb[:, :], ps_y[:, 2 * P:3 * P]).then_inc(out_copied, 1)

            rounds(dve, one_round)


_INS = ["r_target_item", "r_history_sequence", "r_mask",
        "L0_rec_W_q", "L0_rec_W_k", "L0_rec_W_v", "L0_rec_W_o"]


def kernel(**inputs):
    import numpy as np
    import concourse.bacc as bacc
    from concourse.bass_utils import run_bass_kernel_spmd

    nc = bacc.Bacc("TRN2", target_bir_lowering=False, num_devices=1)
    arrays, args = {}, []
    for name in _INS:
        a = np.asarray(inputs[name])
        if name == "r_mask":
            a = a.reshape(-1, 4, 4, 2, a.shape[1]).transpose(0, 2, 1, 3, 4).reshape(a.shape)
        a = np.ascontiguousarray(a)
        arrays[name] = a
        args.append(nc.dram_tensor(name, a.shape, mybir.dt.from_np(a.dtype), kind="ExternalInput").ap())
    out = nc.dram_tensor("out", arrays["r_target_item"].shape, F32, kind="ExternalOutput").ap()
    target_attention(nc, *args, out)
    return run_bass_kernel_spmd(nc, [arrays], core_ids=[0]).results[0]["out"]
```

```python
from contextlib import ExitStack

import concourse.bass as bass
from concourse import mybir

ALU = mybir.AluOpType
ACT = mybir.ActivationFunctionType
F32 = mybir.dt.float32
I32 = mybir.dt.int32


def target_attention(nc, target, history, mask, w_q, w_k, w_v, w_o, out):
    B, S, D = history.shape
    P = 128
    H = 4
    HD = D // H
    HALF = S // 2
    SPLIT = 96
    TILES = 4
    PAIR = 2
    QUAD = 4
    STEP = TILES * PAIR
    STEPS = 4
    GROUPS = 4
    GROUP = STEP * STEPS
    SLOTS = STEPS * GROUPS
    ROUND = GROUP * GROUPS
    ROUNDS = B // ROUND
    BLOCK = 32
    TURNED = STEPS - 1
    BANKS = STEP // 2
    LAG_S = 1
    LAG_C = 6
    TAIL = 9
    NEG = 1e9
    INV_SCALE = float(HD) ** -0.5
    assert D == P and H * GROUP == P and HALF <= P and B % ROUND == 0

    history_v = history.rearrange("b (p t) d -> p b (t d)", t=2)

    with ExitStack() as ctx:
        def sb(name, shape, dt=F32):
            return ctx.enter_context(nc.sbuf_tensor(name, shape, dt))

        def ps(name, shape):
            return ctx.enter_context(nc.psum_tensor(name, shape, F32))

        def sem(name):
            return ctx.enter_context(nc.semaphore(name))

        hist = sb("hist", [P, SLOTS, STEP, 2, D])
        hist_t = [sb(f"hist_t{i}", [P, STEP, S]) for i in range(2)]
        hist_x = sb("hist_x", [P, STEP, S])
        blocks = [sb(f"blocks{i}", [P, STEP * 2, D]) for i in range(2)]
        u_pad = [sb(f"u_pad{i}", [P, STEPS, TILES, 32]) for i in range(2)]
        p_pad = [sb(f"p_pad{i}", [P, 2, STEPS // 2, TILES, 32]) for i in range(2)]
        x_sb = sb("x_sb", [P, D])
        x_t = sb("x_t", [P, ROUND])
        u_sb = sb("u_sb", [P, ROUND, H])
        pair_sel = sb("pair_sel", [P, PAIR])
        quad_sel = sb("quad_sel", [P, QUAD])
        sel_sum = sb("sel_sum", [P, PAIR])
        mask_sb = [sb(f"mask{g}", [P, S], I32) for g in range(GROUPS)]
        keep = [sb(f"keep{i}", [P, S]) for i in range(2)]
        fill = [sb(f"fill{i}", [P, S]) for i in range(2)]
        half_score = sb("half_score", [P, S])
        full_score = sb("full_score", [P, S])
        kept = sb("kept", [P, S])
        neg_score = sb("neg_score", [P, S])
        neg_max = sb("neg_max", [P, 1])
        probs = sb("probs", [P, S])
        row_sum = sb("row_sum", [P, 1])
        inv_sum = sb("inv_sum", [P, 1])
        quad_inv = sb("quad_inv", [P, QUAD])
        ctx_part = [sb(f"ctx_part{i}", [P, D]) for i in range(QUAD - 1)]
        ctx_sb = sb("ctx_sb", [P, D])
        ctx_t = sb("ctx_t", [P, H, ROUND])
        out_sb = sb("out_sb", [ROUND, D])
        w_in = sb("w_in", [P, 4, P])
        w_t = sb("w_t", [P, 2, P])
        w_qk = sb("w_qk", [P, H, P])
        values_t = sb("values_t", [P, ROUND])
        ident = sb("ident", [P, P])

        ps_t = [ps(f"ps_t{q}", [P, 512]) for q in range(BANKS)]
        ps_s = ps("ps_s", [P, 512])
        ps_c = ps("ps_c", [P, 512])
        ps_p = ps("ps_p", [P, 512])
        ps_y = ps("ps_y", [P, 512])

        w_loaded = sem("w_loaded")
        x_loaded = sem("x_loaded")
        hist_loaded = [sem(f"hist_loaded{s}") for s in range(SLOTS)]
        mask_loaded = [sem(f"mask_loaded{g}") for g in range(GROUPS)]
        out_stored = sem("out_stored")
        zeroed = sem("zeroed")
        ident_ready = sem("ident_ready")
        u_pad_zero = sem("u_pad_zero")
        p_pad_zero = sem("p_pad_zero")
        w_t_done = sem("w_t_done")
        w_t_copied = sem("w_t_copied")
        w_qk_done = sem("w_qk_done")
        w_qk_act = sem("w_qk_act")
        w_qk_dve = sem("w_qk_dve")
        x_t_done = sem("x_t_done")
        x_t_copied = sem("x_t_copied")
        u_done = sem("u_done")
        u_copied = sem("u_copied")
        banks_done = sem("banks_done")
        even_copied = sem("even_copied")
        odd_copied = sem("odd_copied")
        rows_zero = sem("rows_zero")
        blocks_ready = sem("blocks_ready")
        x_moved_act = sem("x_moved_act")
        x_moved_dve = sem("x_moved_dve")
        u_pad_ready = sem("u_pad_ready")
        fill_ready = sem("fill_ready")
        mask_ready = sem("mask_ready")
        scores_done = sem("scores_done")
        sel_ready = sem("sel_ready")
        half_ready = sem("half_ready")
        scores_read = sem("scores_read")
        kept_ready = sem("kept_ready")
        masked = sem("masked")
        max_ready = sem("max_ready")
        exp_done = sem("exp_done")
        inv_ready = sem("inv_ready")
        probs_t_done = sem("probs_t_done")
        p_pad_ready = sem("p_pad_ready")
        ctx_done = sem("ctx_done")
        quad_inv_ready = sem("quad_inv_ready")
        ctx_part_ready = sem("ctx_part_ready")
        ctx_copied = sem("ctx_copied")
        ctx_t_done = sem("ctx_t_done")
        ctx_t_copied = sem("ctx_t_copied")
        values_done = sem("values_done")
        values_copied = sem("values_copied")
        out_done = sem("out_done")
        out_copied = sem("out_copied")

        block = ctx.enter_context(nc.Block())

        def wait(eng, semaphore, rnd, per_round, offset):
            count = rnd * per_round + offset
            if isinstance(rnd, int):
                if count > 0:
                    eng.wait_ge(semaphore, count)
            else:
                assert per_round + offset > 0
                eng.wait_ge(semaphore, count)

        def rounds(eng, one_round, looks_ahead=False):
            one_round(0, range(SLOTS), True, False)
            with eng.Fori(1, ROUNDS - looks_ahead) as rnd:
                one_round(rnd, range(SLOTS), False, False)
            if looks_ahead:
                one_round(ROUNDS - 1, range(SLOTS), False, False)
            one_round(ROUNDS, range(TAIL), False, True)

        def pad_columns(pad, shares, width):
            return bass.AP(pad.tensor, pad.offset,
                           [list(pad.ap[0]), [32 * TILES + width, shares], [32, TILES], [1, width]])

        def turned_block(group, a, c, rows):
            return blocks[group % 2][BLOCK * a:BLOCK * (a + 1), :, BLOCK * c:BLOCK * c + rows]

        def moved(c, a, rows):
            part = hist_x[BLOCK * c:BLOCK * (c + 1)].rearrange("p j (t q) -> p (j t) q", t=2)
            return part[:, :, BLOCK * a:BLOCK * a + rows]

        @block.sync
        def _(sp):
            for n, w in enumerate((w_q, w_k, w_v, w_o)):
                sp.dma_start(w_in[:, n, :], w).then_inc(w_loaded, 16)

            def one_round(rnd, slots, first, tail):
                if tail:
                    return
                wait(sp, x_t_done, rnd, 1, 0)
                sp.dma_start(x_sb[:, :], target[bass.ds(rnd * ROUND, ROUND), :]).then_inc(x_loaded, 16)
                for s in slots:
                    gr, k = divmod(s, STEPS)
                    wait(sp, ctx_done, rnd, SLOTS // 2, s // 2 + 1 - SLOTS // 2)
                    if first and k == STEPS - 1:
                        sp.wait_ge(rows_zero, gr + 1)
                    for a, b in ((0, SPLIT), (SPLIT, HALF)):
                        sp.dma_start(
                            hist[a:b, s].rearrange("p b t d -> p b (t d)"),
                            history_v[a:b, bass.ds(rnd * ROUND + s * STEP, STEP), :],
                        ).then_inc(hist_loaded[s], 16)
                    if k == 0:
                        wait(sp, mask_ready, rnd, GROUPS, gr + 1 - GROUPS)
                        rows = mask[bass.ds(rnd * ROUND + gr * GROUP, GROUP), :]
                        sp.dma_start(mask_sb[gr][:, :],
                                     rows.unsqueeze(1).broadcast_to([GROUP, H, S])).then_inc(mask_loaded[gr], 16)

            rounds(sp, one_round)
            sp.wait_ge(out_stored, 16 * ROUNDS)

        @block.gpsimd
        def _(pool):
            pool.memset(ident[:, :], 0.0).then_inc(zeroed, 1)
            pool.wait_ge(zeroed, 1)
            pool.affine_select(out=ident[:, :], in_=ident[:, :], compare_op=ALU.not_equal, fill=1.0,
                               base=0, pattern=[[-1, P]], channel_multiplier=1).then_inc(ident_ready, 1)
            pool.wait_ge(ident_ready, 1)
            for n, s in enumerate(range(STEPS - 1, SLOTS, STEPS)):
                if n:
                    pool.wait_ge(rows_zero, n)
                pool.memset(hist[P - BLOCK:P, s], 0.0).then_inc(rows_zero, 1)
            pool.wait_ge(rows_zero, GROUPS)
            for pad in u_pad:
                pool.memset(pad[:, :, :, :], 0.0).then_inc(u_pad_zero, 1)
            def one_round(rnd, slots, first, tail):
                for s in slots:
                    if (s == 2 * STEPS + 1 or (tail and s == TAIL - 1)) and not first:
                        wait(pool, out_copied, rnd, 1, 0)
                        pool.dma_start(out[bass.ds((rnd - 1) * ROUND, ROUND), :],
                                       out_sb[:, :]).then_inc(out_stored, 16)

            rounds(pool, one_round)

        @block.tensor
        def _(pe):
            pe.wait_ge(ident_ready, 1)
            pe.wait_ge(w_loaded, 64)
            for n in range(2):
                mm = pe.transpose(ps_p[:, n * P:(n + 1) * P], w_in[:, n, :], ident[:, :])
            mm.then_inc(w_t_done, 1)
            pe.wait_ge(w_t_copied, 1)
            for h in range(H):
                rows = slice(h * HD, (h + 1) * HD)
                pe.matmul(ps_t[h][:, 0:P], w_t[rows, 0, :], w_t[rows, 1, :],
                          start=True, stop=True).then_inc(w_qk_done, 1)

            def one_round(rnd, slots, first, tail):
                for s in slots:
                    gr, k = divmod(s, STEPS)
                    if s == 0 and not tail:
                        wait(pe, x_loaded, rnd, 16, 16)
                        wait(pe, ctx_t_copied, rnd, PAIR * GROUPS, -2 * PAIR)
                        pe.transpose(ps_y[:, 0:ROUND], x_sb[:, :], ident[:, :]).then_inc(x_t_done, 1)
                    ts = TURNED * gr + k
                    if not tail and k < TURNED:
                        wait(pe, hist_loaded[s], rnd, 32, 32)
                        for q in range(BANKS):
                            if first and s == 0:
                                pe.wait_ge(w_qk_act if q % 2 == 0 else w_qk_dve, 2)
                            wait(pe, even_copied if q % 2 == 0 else odd_copied, rnd,
                                 2 * TURNED * GROUPS, 2 * (ts - 1) + q // 2 + 1)
                            for j in (2 * q, 2 * q + 1):
                                for t in range(2):
                                    at = (j % 2) * S + t * HALF
                                    mm = pe.transpose(ps_t[q][:, at:at + HALF], hist[0:HALF, s, j, t, :],
                                                      ident[0:HALF, 0:HALF])
                            mm.then_inc(banks_done, 1)
                    if s == 0 and not tail:
                        wait(pe, x_t_copied, rnd, 1, 1)
                        wait(pe, p_pad_ready, rnd, 2 * GROUPS, -2)
                        for h in range(H):
                            mm = pe.matmul(ps_p[:, h * ROUND:(h + 1) * ROUND], w_qk[:, h, :],
                                           x_t[:, :], start=True, stop=True)
                        mm.then_inc(u_done, 1)
                    if s == STEPS + 3 and not first:
                        wait(pe, ctx_t_copied, rnd, PAIR * GROUPS, 0)
                        for h in range(H):
                            mm = pe.matmul(ps_y[h * HD:(h + 1) * HD, 2 * P:3 * P],
                                           w_in[:, 2, h * HD:(h + 1) * HD], ctx_t[:, h, :],
                                           start=True, stop=True)
                        mm.then_inc(values_done, 1)
                    if s == STEPS + 4 and not first:
                        wait(pe, values_copied, rnd, 1, 0)
                        pe.matmul(ps_y[:, 3 * P:4 * P], values_t[:, :], w_in[:, 3, :],
                                  start=True, stop=True).then_inc(out_done, 1)
                    if not (first and s < LAG_S) and not (tail and s >= LAG_S):
                        m = (s - LAG_S) % SLOTS
                        mg, mk = divmod(m, STEPS)
                        source = hist_t[mk % 2]
                        if mk < TURNED:
                            wait(pe, even_copied, rnd, 2 * TURNED * GROUPS, 2 * (TURNED * mg + mk + 1))
                            wait(pe, odd_copied, rnd, 2 * TURNED * GROUPS, 2 * (TURNED * mg + mk + 1))
                        else:
                            source = hist_x
                            of = mg + 1 - (GROUPS if s < LAG_S else 0)
                            wait(pe, x_moved_act, rnd, 12 * GROUPS, 12 * of)
                            wait(pe, x_moved_dve, rnd, 4 * GROUPS, 4 * of)
                        if mk == 0:
                            wait(pe, u_pad_ready, rnd, GROUPS, mg + 1)
                            wait(pe, scores_read, rnd, GROUPS, mg)
                        for g in range(TILES):
                            mm = pe.matmul(ps_s[32 * g:32 * g + 32, 0:PAIR * S], u_pad[mg % 2][:, mk, g, :],
                                           source[:, PAIR * g:PAIR * (g + 1), :],
                                           start=(mk == 0), stop=(mk == STEPS - 1))
                        mm.then_inc(scores_done, 1)
                    if k == 1 and not (first and gr == 0) and not (tail and gr > 0):
                        wait(pe, exp_done, rnd, GROUPS, gr)
                        if gr == 0 and not tail:
                            wait(pe, u_copied, rnd, 1, 1)
                        else:
                            wait(pe, p_pad_ready, rnd, 2 * GROUPS, 2 * (gr - 1))
                        for t in range(2):
                            mm = pe.transpose(ps_p[0:HALF, t * P:(t + 1) * P],
                                              probs[:, t * HALF:(t + 1) * HALF], ident[:, :])
                        mm.then_inc(probs_t_done, 1)
                    if k == 2 and not (first and gr < 2):
                        wait(pe, ctx_copied, rnd, GROUPS, gr - 1)
                        if gr == 0 and not tail:
                            wait(pe, x_t_copied, rnd, 1, 1)
                        elif gr == 2:
                            wait(pe, out_copied, rnd, 1, 0)
                        else:
                            wait(pe, ctx_t_copied, rnd, PAIR * GROUPS, PAIR * (gr - 2))
                        pe.transpose(ps_y[:, P:2 * P], ctx_sb[:, :], ident[:, :]).then_inc(ctx_t_done, 1)
                    if s % 2 == 0 and not (first and s < LAG_C) and not (tail and s >= LAG_C):
                        m = (s - LAG_C) % SLOTS
                        mg, mk = divmod(m, STEPS)
                        behind = GROUPS if s < LAG_C else 0
                        if mk == 0:
                            wait(pe, p_pad_ready, rnd, 2 * GROUPS, 2 * (mg + 1 - behind))
                            wait(pe, ctx_copied, rnd, GROUPS, mg - behind)
                        for t in range(2):
                            for g in range(TILES):
                                mm = pe.matmul(ps_c[32 * g:32 * g + 32, :],
                                               p_pad[mg % 2][0:HALF, t, mk // 2, g, :],
                                               hist[0:HALF, m:m + 2, PAIR * g:PAIR * (g + 1), t, :],
                                               start=(mk == 0 and t == 0),
                                               stop=(mk == STEPS - 2 and t == 1))
                        mm.then_inc(ctx_done, 1)

            rounds(pe, one_round)

        @block.scalar
        def _(act):
            act.wait_ge(w_t_done, 1)
            act.copy(w_t[:, :, :], ps_p[:, 0:2 * P].rearrange("p (n c) -> p n c", n=2)).then_inc(w_t_copied, 1)
            for h in (0, 2):
                act.wait_ge(w_qk_done, h + 1)
                act.copy(w_qk[:, h, :], ps_t[h][:, 0:P]).then_inc(w_qk_act, 1)

            def one_round(rnd, slots, first, tail):
                for s in slots:
                    gr, k = divmod(s, STEPS)
                    if s == 0 and not tail:
                        wait(act, x_t_done, rnd, 1, 1)
                        wait(act, u_done, rnd, 1, 0)
                        act.copy(x_t[:, :], ps_y[:, 0:ROUND]).then_inc(x_t_copied, 1)
                    ts = TURNED * gr + k
                    if not tail and k < TURNED:
                        for q in (0, 2):
                            wait(act, banks_done, rnd, BANKS * TURNED * GROUPS, BANKS * ts + q + 1)
                            wait(act, scores_done, rnd, SLOTS, s - 1)
                            act.copy(hist_t[k % 2][:, 2 * q:2 * q + 2, :],
                                     ps_t[q][:, 0:2 * S].rearrange("p (j c) -> p j c", j=2)
                                     ).then_inc(even_copied, 1)
                    if s == 0 and not tail:
                        wait(act, u_done, rnd, 1, 1)
                        wait(act, u_pad_ready, rnd, GROUPS, 0)
                        act.copy(u_sb[:, :, :],
                                 ps_p[:, :].rearrange("p (h b) -> p b h", h=H)).then_inc(u_copied, 1)
                    if not tail:
                        for a, c in [(a, c) for a in range(3) for c in range(4)][3 * k:3 * k + 3]:
                            wait(act, blocks_ready, rnd, BANKS * GROUPS, BANKS * (gr + 1))
                            wait(act, scores_done, rnd, SLOTS, s - k)
                            act.copy(
                                moved(c, a, BLOCK), turned_block(gr, a, c, BLOCK),
                            ).then_inc(x_moved_act, 1)
                    if k == 0 and not (first and gr == 0) and not (tail and gr > 0):
                        wait(act, max_ready, rnd, GROUPS, gr)
                        wait(act, probs_t_done, rnd, GROUPS, gr - 1)
                        wait(act, inv_ready, rnd, GROUPS, gr - 1)
                        act.activation(probs[:, :], neg_score[:, :], ACT.Exp, bias=neg_max[:, 0:1],
                                       scale=-1.0, accum_out=row_sum[:, 0:1]).then_inc(exp_done, 1)
                    if s == STEPS + 3 and not first:
                        wait(act, values_done, rnd, 1, 0)
                        act.copy(values_t[:, :], ps_y[:, 2 * P:3 * P]).then_inc(values_copied, 1)
                    if k == 2 and not (first and gr < 2):
                        g_of = (gr - 2) % GROUPS
                        wait(act, ctx_t_done, rnd, GROUPS, gr - 1)
                        if g_of == 0:
                            wait(act, values_done, rnd, 1, 0)
                        of_group = ctx_t[:, :, g_of * GROUP:(g_of + 1) * GROUP]
                        of_group = of_group.rearrange("p h (k g e) -> p e h g k", g=TILES, e=PAIR)
                        turned = ps_y[:, P:2 * P].rearrange("p (g k e h) -> p e h g k", g=TILES, e=PAIR, h=H)
                        for e in range(PAIR):
                            act.copy(of_group[:, e], turned[:, e]).then_inc(ctx_t_copied, 1)


            rounds(act, one_round)

        @block.vector
        def _(dve):
            for pad in p_pad:
                dve.memset(pad[:, :, :, :, :], 0.0).then_inc(p_pad_zero, 1)
            dve.wait_ge(p_pad_zero, 2)
            dve.wait_ge(u_pad_zero, 2)
            dve.wait_ge(ident_ready, 1)
            dve.tensor_reduce(quad_sel[:, :], ident[:, :].rearrange("p (a c h) -> p c a h", c=QUAD, h=H),
                              mybir.AxisListType.XY, ALU.add).then_inc(sel_ready, 1)
            dve.tensor_reduce(sel_sum[:, :], ident[:, :].rearrange("p (a e h) -> p e a h", e=PAIR, h=H),
                              mybir.AxisListType.XY, ALU.add).then_inc(sel_ready, 1)
            dve.wait_ge(sel_ready, 2)
            dve.tensor_scalar(pair_sel[:, :], sel_sum[:, :], -INV_SCALE, None, ALU.mult).then_inc(sel_ready, 1)
            dve.wait_ge(sel_ready, 3)
            for h in (1, 3):
                dve.wait_ge(w_qk_done, h + 1)
                dve.tensor_copy(w_qk[:, h, :], ps_t[h][:, 0:P]).then_inc(w_qk_dve, 1)

            def turn_blocks(rnd, group, pieces):
                rnd, group = rnd + group // GROUPS, group % GROUPS
                if isinstance(rnd, int) and rnd == ROUNDS:
                    return
                slot = group * STEPS + STEPS - 1
                wait(dve, x_moved_act, rnd, 12 * GROUPS, 12 * (group - 1))
                wait(dve, x_moved_dve, rnd, 4 * GROUPS, 4 * (group - 1))
                wait(dve, hist_loaded[slot], rnd, 32, 32)
                for n in pieces:
                    dve.transpose(
                        blocks[group % 2][:, 4 * n:4 * n + 4, :].rearrange("p j d -> p (j d)"),
                        hist[:, slot, 2 * n:2 * n + 2].rearrange("p j t d -> p (j t d)"),
                    ).then_inc(blocks_ready, 1)

            def one_round(rnd, slots, first, tail):
                for s in slots:
                    gr, k = divmod(s, STEPS)
                    ts = TURNED * gr + k
                    if not tail and k < TURNED:
                        for q in (1, 3):
                            wait(dve, banks_done, rnd, BANKS * TURNED * GROUPS, BANKS * ts + q + 1)
                            wait(dve, scores_done, rnd, SLOTS, s - 1)
                            dve.tensor_copy(hist_t[k % 2][:, 2 * q:2 * q + 2, :],
                                            ps_t[q][:, 0:2 * S].rearrange("p (j c) -> p j c", j=2)
                                            ).then_inc(odd_copied, 1)
                    if not tail and (s == 0 or (k == 2 and gr < GROUPS - 1)):
                        ug = 0 if s == 0 else gr + 1
                        wait(dve, scores_done, rnd, SLOTS, STEPS * (ug - 1))
                        if s == 0:
                            wait(dve, u_copied, rnd, 1, 1)
                        dve.tensor_copy(
                            pad_columns(u_pad[ug % 2][:, :, :, :], STEPS, 8),
                            u_sb[:, ug * GROUP:(ug + 1) * GROUP, :].rearrange(
                                "p (k g e) h -> p k g (e h)", g=TILES, e=PAIR),
                        ).then_inc(u_pad_ready, 1)
                    if k == 0 and not (first and gr == 0) and not (tail and gr > 0):
                        par = (gr - 1) % 2
                        wait(dve, scores_done, rnd, SLOTS, STEPS * gr)
                        wait(dve, mask_ready, rnd, GROUPS, gr)
                        wait(dve, scores_read, rnd, GROUPS, gr - 1)
                        dve.tensor_scalar(half_score[:, :], ps_s[:, 0:S], pair_sel[:, 0:1], None,
                                          ALU.mult).then_inc(half_ready, 1)
                        wait(dve, kept_ready, rnd, GROUPS, gr - 1)
                        wait(dve, half_ready, rnd, GROUPS, gr)
                        dve.scalar_tensor_tensor(full_score[:, :], ps_s[:, S:2 * S], pair_sel[:, 1:2],
                                                 half_score[:, :], ALU.mult,
                                                 ALU.add).then_inc(scores_read, 1)
                        wait(dve, masked, rnd, GROUPS, gr - 1)
                        wait(dve, scores_read, rnd, GROUPS, gr)
                        dve.tensor_tensor(kept[:, :], full_score[:, :], keep[par][:, :],
                                          ALU.mult).then_inc(kept_ready, 1)
                        wait(dve, exp_done, rnd, GROUPS, gr - 1)
                        wait(dve, kept_ready, rnd, GROUPS, gr)
                        dve.tensor_tensor(neg_score[:, :], kept[:, :], fill[par][:, :],
                                          ALU.add).then_inc(masked, 1)
                        wait(dve, masked, rnd, GROUPS, gr)
                        dve.tensor_reduce(neg_max[:, 0:1], neg_score[:, :], mybir.AxisListType.X,
                                          ALU.min).then_inc(max_ready, 1)
                    if k == 1 and not (first and gr < 2):
                        wait(dve, ctx_part_ready, rnd, GROUPS * (QUAD - 1), (QUAD - 1) * (gr - 2))
                        wait(dve, ctx_copied, rnd, GROUPS, gr - 2)
                        wait(dve, inv_ready, rnd, GROUPS, gr - 1)
                        dve.tensor_scalar(quad_inv[:, :], quad_sel[:, :], inv_sum[:, 0:1], None,
                                          ALU.mult).then_inc(quad_inv_ready, 1)
                        wait(dve, quad_inv_ready, rnd, GROUPS, gr - 1)
                        wait(dve, ctx_done, rnd, SLOTS // 2, STEPS // 2 * (gr - 1))
                        dve.tensor_scalar(ctx_part[0][:, :], ps_c[:, 0:D], quad_inv[:, 0:1], None,
                                          ALU.mult).then_inc(ctx_part_ready, 1)
                        for c in range(1, QUAD):
                            last = c == QUAD - 1
                            if last:
                                wait(dve, ctx_t_done, rnd, GROUPS, gr - 2)
                            wait(dve, ctx_part_ready, rnd, GROUPS * (QUAD - 1), (QUAD - 1) * (gr - 2) + c)
                            dve.scalar_tensor_tensor(
                                (ctx_sb if last else ctx_part[c])[:, :], ps_c[:, c * D:(c + 1) * D],
                                quad_inv[:, c:c + 1], ctx_part[c - 1][:, :], ALU.mult, ALU.add,
                            ).then_inc(ctx_copied if last else ctx_part_ready, 1)
                    if k == 1 and not (first and gr == 0) and not (tail and gr > 0):
                        par = (gr - 1) % 2
                        wait(dve, exp_done, rnd, GROUPS, gr)
                        wait(dve, quad_inv_ready, rnd, GROUPS, gr - 1)
                        dve.reciprocal(inv_sum[:, :], row_sum[:, :]).then_inc(inv_ready, 1)
                        wait(dve, ctx_done, rnd, SLOTS // 2, STEPS // 2 * (gr - 2))
                        wait(dve, probs_t_done, rnd, GROUPS, gr)
                        for t in range(2):
                            dve.tensor_copy(
                                pad_columns(p_pad[par][0:HALF, t], STEPS // 2, 16),
                                ps_p[0:HALF, t * P:(t + 1) * P].rearrange("p (g n c) -> p n g c", g=TILES, c=16),
                            ).then_inc(p_pad_ready, 1)
                    if k == 3 and not tail:
                        wait(dve, max_ready, rnd, GROUPS, gr - 1)
                        wait(dve, mask_loaded[gr], rnd, 16, 16)
                        dve.tensor_scalar(fill[gr % 2][:, :].rearrange("p (t q) -> p t q", t=2),
                                          mask_sb[gr][:, :].rearrange("p (q t) -> p t q", t=2),
                                          0.0, NEG, ALU.is_equal, ALU.mult).then_inc(fill_ready, 1)
                        wait(dve, fill_ready, rnd, GROUPS, gr + 1)
                        dve.tensor_scalar(keep[gr % 2][:, :], fill[gr % 2][:, :], 0.5, None,
                                          ALU.is_lt).then_inc(mask_ready, 1)
                    if not tail:
                        if first and s == 0:
                            turn_blocks(rnd, 0, range(BANKS))
                        if k != 1:
                            turn_blocks(rnd, gr + 1, {0: (0,), 2: (1,), 3: (2, 3)}[k])
                        if k == 2:
                            wait(dve, blocks_ready, rnd, BANKS * GROUPS, BANKS * (gr + 1))
                            wait(dve, scores_done, rnd, SLOTS, s - k)
                            for c in range(4):
                                dve.tensor_copy(moved(c, 3, HALF - 3 * BLOCK),
                                                turned_block(gr, 3, c, HALF - 3 * BLOCK)).then_inc(x_moved_dve, 1)
                    if s == SLOTS - 1 and not first:
                        wait(dve, out_stored, rnd, 16, 0)
                    if s == STEPS + 4 and not first:
                        wait(dve, out_done, rnd, 1, 0)
                        dve.tensor_copy(out_sb[:, :], ps_y[:, 3 * P:4 * P]).then_inc(out_copied, 1)

            rounds(dve, one_round, looks_ahead=True)


_INS = ["r_target_item", "r_history_sequence", "r_mask",
        "L0_rec_W_q", "L0_rec_W_k", "L0_rec_W_v", "L0_rec_W_o"]


def kernel(**inputs):
    import numpy as np
    import concourse.bacc as bacc
    from concourse.bass_utils import run_bass_kernel_spmd

    nc = bacc.Bacc("TRN2", target_bir_lowering=False, num_devices=1)
    arrays, args = {}, []
    for name in _INS:
        a = np.asarray(inputs[name])
        if name == "r_mask":
            a = a.reshape(-1, 4, 4, 2, a.shape[1]).transpose(0, 2, 1, 3, 4).reshape(a.shape)
        a = np.ascontiguousarray(a)
        arrays[name] = a
        args.append(nc.dram_tensor(name, a.shape, mybir.dt.from_np(a.dtype), kind="ExternalInput").ap())
    out = nc.dram_tensor("out", arrays["r_target_item"].shape, F32, kind="ExternalOutput").ap()
    target_attention(nc, *args, out)
    return run_bass_kernel_spmd(nc, [arrays], core_ids=[0]).results[0]["out"]
```

```python
from contextlib import ExitStack

import concourse.bass as bass
from concourse import mybir

ALU = mybir.AluOpType
ACT = mybir.ActivationFunctionType
F32 = mybir.dt.float32
I32 = mybir.dt.int32


def target_attention(nc, target, history, mask, w_q, w_k, w_v, w_o, out):
    B, S, D = history.shape
    P = 128
    H = 4
    HD = D // H
    HALF = S // 2
    SPLIT = 96
    TILES = 4
    PAIR = 2
    QUAD = 4
    STEP = TILES * PAIR
    STEPS = 4
    GROUPS = 4
    GROUP = STEP * STEPS
    SLOTS = STEPS * GROUPS
    ROUND = GROUP * GROUPS
    ROUNDS = B // ROUND
    BLOCK = 32
    TURNED = (3, 6, 9, 12, 15)
    BLOCKS_IN = (0, 1, 0, 1, 2)
    MOVED_TO = (0, 1, 0, 1, 0)
    TURNS = (1, 1, 0, 4, 0, 1, 2, 0, 1, 3, 2, 0, 1, 0, 3, 1)
    TURNS_FIRST = (0, 0, 0, 4, 0, 0, 2, 0, 0, 1, 0, 0, 1, 0, 0, 0)
    MOVES = (3, 5, 0, 5, 2, 3, 6, 1, 8, 0, 5, 3, 3, 4, 3, 4)
    MOVES_FIRST = (0, 0, 0, 0, 0, 1, 2, 1, 0, 0, 0, 1, 1, 0, 1, 0)
    BEFORE = (3, 3, 0, 3, 2, 3, 4, 1, 5, 0, 0, 2, 3, 3, 3, 4)
    DVE_MOVES = {2: 3, 5: 6, 7: 9, 12: 12, 14: 15}
    BY_ACT = 11
    BY_DVE = 5
    CTX_FIRST = (2, 3, 3, 1)
    BANKS = STEP // 2
    TURN_FIRST = (2,)
    SPLIT_PRODUCTS = (12,)
    PIECES = STEP // 2
    LAG_S = 1
    LAG_C = 6
    TAIL = 9
    NEG = 1e9
    INV_SCALE = float(HD) ** -0.5
    assert D == P and H * GROUP == P and HALF <= P and B % ROUND == 0

    history_v = history.rearrange("b (p t) d -> p b (t d)", t=2)

    with ExitStack() as ctx:
        def sb(name, shape, dt=F32):
            return ctx.enter_context(nc.sbuf_tensor(name, shape, dt))

        def ps(name, shape):
            return ctx.enter_context(nc.psum_tensor(name, shape, F32))

        def sem(name):
            return ctx.enter_context(nc.semaphore(name))

        hist = sb("hist", [P, SLOTS, STEP, 2, D])
        hist_t = [sb(f"hist_t{i}", [P, STEP, S]) for i in range(2)]
        hist_x = [sb(f"hist_x{i}", [P, STEP, S]) for i in range(2)]
        blocks = [sb(f"blocks{i}", [P, STEP * 2, D]) for i in range(3)]
        u_pad = [sb(f"u_pad{i}", [P, STEPS, TILES, 32]) for i in range(2)]
        p_pad = [sb(f"p_pad{i}", [P, 2, STEPS // 2, TILES, 32]) for i in range(2)]
        x_sb = sb("x_sb", [P, D])
        x_t = sb("x_t", [P, ROUND])
        u_sb = sb("u_sb", [P, ROUND, H])
        pair_sel = sb("pair_sel", [P, PAIR])
        quad_sel = sb("quad_sel", [P, QUAD])
        mask_sb = [sb(f"mask{g}", [P, S], I32) for g in range(GROUPS)]
        mask_odd = sb("mask_odd", [P, S], I32)
        neg_score = sb("neg_score", [P, S])
        carrier = sb("carrier", [1, 2])
        neg_max = sb("neg_max", [P, 1])
        probs = sb("probs", [P, S])
        row_sum = sb("row_sum", [P, 1])
        inv_sum = sb("inv_sum", [P, 1])
        quad_inv = sb("quad_inv", [P, QUAD])
        ctx_part = [sb(f"ctx_part{i}", [P, D]) for i in range(QUAD - 1)]
        ctx_sb = sb("ctx_sb", [P, D])
        ctx_t = sb("ctx_t", [P, H, ROUND])
        out_sb = sb("out_sb", [ROUND, D])
        w_in = sb("w_in", [P, 4, P])
        w_t = sb("w_t", [P, 2, P])
        w_qk = sb("w_qk", [P, H, P])
        values_t = sb("values_t", [P, ROUND])
        ident = sb("ident", [P, P])

        ps_t = ps("ps_t", [P, BANKS, 512])
        ps_s = ps("ps_s", [P, 512])
        ps_c = ps("ps_c", [P, 512])
        ps_p = ps("ps_p", [P, 512])
        ps_y = ps("ps_y", [P, 512])

        w_qk_loaded = sem("w_qk_loaded")
        w_vo_loaded = sem("w_vo_loaded")
        x_loaded = sem("x_loaded")
        hist_loaded = [sem(f"hist_loaded{s}") for s in range(SLOTS)]
        mask_loaded = [sem(f"mask_loaded{g}") for g in range(GROUPS)]
        out_stored = sem("out_stored")
        zeroed = sem("zeroed")
        ident_ready = sem("ident_ready")
        u_pad_zero = sem("u_pad_zero")
        p_pad_zero = sem("p_pad_zero")
        w_t_done = sem("w_t_done")
        w_t_copied = sem("w_t_copied")
        w_qk_done = sem("w_qk_done")
        w_qk_act = sem("w_qk_act")
        w_qk_dve = sem("w_qk_dve")
        x_t_done = sem("x_t_done")
        x_t_copied = sem("x_t_copied")
        u_done = sem("u_done")
        u_copied = sem("u_copied")
        low_done = sem("low_done")
        high_done = sem("high_done")
        low_copied = sem("low_copied")
        high_copied = sem("high_copied")
        rows_zero = sem("rows_zero")
        blocks_ready = sem("blocks_ready")
        x_moved_act = sem("x_moved_act")
        x_moved_dve = sem("x_moved_dve")
        u_pad_ready = sem("u_pad_ready")
        mask_odd_ready = sem("mask_odd_ready")
        filled = sem("filled")
        scores_done = sem("scores_done")
        sel_ready = sem("sel_ready")
        first_read = sem("first_read")
        scores_read = sem("scores_read")
        max_ready = sem("max_ready")
        exp_done = sem("exp_done")
        inv_ready = sem("inv_ready")
        probs_t_done = sem("probs_t_done")
        p_pad_ready = sem("p_pad_ready")
        ctx_done = sem("ctx_done")
        quad_inv_ready = sem("quad_inv_ready")
        ctx_part_ready = sem("ctx_part_ready")
        ctx_copied = sem("ctx_copied")
        ctx_t_done = sem("ctx_t_done")
        ctx_t_copied = sem("ctx_t_copied")
        values_done = sem("values_done")
        values_copied = sem("values_copied")
        out_done = sem("out_done")
        out_copied = sem("out_copied")

        block = ctx.enter_context(nc.Block())

        def wait(eng, semaphore, rnd, per_round, offset):
            count = rnd * per_round + offset
            if isinstance(rnd, int):
                if count > 0:
                    eng.wait_ge(semaphore, count)
            else:
                assert per_round + offset > 0
                eng.wait_ge(semaphore, count)

        X_ROUND = len(TURNED)
        T_ROUND = SLOTS - X_ROUND

        def is_turned(first, s):
            return s == SLOTS - 1 if first and s < SLOTS else s % SLOTS in TURNED

        def turned_before(first, s):
            if first and s < SLOTS:
                return 0
            over, slot = divmod(s, SLOTS)
            return over * X_ROUND + sum(x < slot for x in TURNED) - (X_ROUND - 1)

        def transposed_before(first, s):
            return s - turned_before(first, s)

        def share(counts, s, per_slot):
            done = sum(counts[:s])
            return [divmod(i, per_slot) for i in range(done, done + counts[s])]

        def to_move(first, s):
            return [(n, i) for n, i in share(MOVES, s, BY_ACT) if is_turned(first, TURNED[n])]

        def to_turn(first, s):
            if first:
                return {12: [(3, i) for i in range(PIECES)], 15: [(4, i) for i in range(PIECES)]}.get(s, [])
            return share(TURNS, s, PIECES)

        def moved_over(first, n):
            return 0 if first else (0, 12 - SLOTS + 1, 3 + 1, 6 + 1, 9 + 1)[n]

        MOVE_ORDER = [(a, c) for a in range(3) for c in range(4)]

        def rounds(eng, one_round, looks_ahead=False):
            one_round(0, range(SLOTS), True, False)
            with eng.Fori(1, ROUNDS - looks_ahead) as rnd:
                one_round(rnd, range(SLOTS), False, False)
            if looks_ahead:
                one_round(ROUNDS - 1, range(SLOTS), False, False)
            one_round(ROUNDS, range(TAIL), False, True)

        def pad_columns(pad, shares, width):
            return bass.AP(pad.tensor, pad.offset,
                           [list(pad.ap[0]), [32 * TILES + width, shares], [32, TILES], [1, width]])

        def two_banks(q):
            return ps_t[:, q:q + 2, 0:2 * S]

        def two_banks_to(buffer, q):
            return buffer[:, 2 * q:2 * q + 4, :].rearrange("p (q j) c -> p q (j c)", q=2)

        def turned_block(slot, a, c, rows):
            return blocks[BLOCKS_IN[TURNED.index(slot)]][BLOCK * a:BLOCK * (a + 1), :, BLOCK * c:BLOCK * c + rows]

        def moved(slot, c, a, rows):
            part = hist_x[MOVED_TO[TURNED.index(slot)]][BLOCK * c:BLOCK * (c + 1)].rearrange("p j (t q) -> p (j t) q", t=2)
            return part[:, :, BLOCK * a:BLOCK * a + rows]

        @block.sync
        def _(sp):
            for n, w in enumerate((w_q, w_k)):
                sp.dma_start(w_in[:, n, :], w).then_inc(w_qk_loaded, 16)

            def one_round(rnd, slots, first, tail):
                if tail:
                    return
                wait(sp, x_t_done, rnd, 1, 0)
                sp.dma_start(x_sb[:, :], target[bass.ds(rnd * ROUND, ROUND), :]).then_inc(x_loaded, 16)
                for s in slots:
                    gr, k = divmod(s, STEPS)
                    wait(sp, ctx_done, rnd, SLOTS // 2, s // 2 + 1 - SLOTS // 2)
                    if first and s in TURNED:
                        sp.wait_ge(rows_zero, TURNED.index(s) + 1)
                    for a, b in ((0, SPLIT), (SPLIT, HALF)):
                        sp.dma_start(
                            hist[a:b, s].rearrange("p b t d -> p b (t d)"),
                            history_v[a:b, bass.ds(rnd * ROUND + s * STEP, STEP), :],
                        ).then_inc(hist_loaded[s], 16)
                    if k == 0:
                        wait(sp, scores_read, rnd, GROUPS, gr + 1 - GROUPS)
                        rows = mask[bass.ds(rnd * ROUND + gr * GROUP, GROUP), :]
                        sp.dma_start(mask_sb[gr][:, :],
                                     rows.unsqueeze(1).broadcast_to([GROUP, H, S])).then_inc(mask_loaded[gr], 16)
                    if first and s == 2:
                        for n, w in ((2, w_v), (3, w_o)):
                            sp.dma_start(w_in[:, n, :], w).then_inc(w_vo_loaded, 16)

            rounds(sp, one_round)
            sp.wait_ge(out_stored, 16 * ROUNDS)

        @block.gpsimd
        def _(pool):
            pool.memset(ident[:, :], 0.0).then_inc(zeroed, 1)
            pool.wait_ge(zeroed, 1)
            pool.affine_select(out=ident[:, :], in_=ident[:, :], compare_op=ALU.not_equal, fill=1.0,
                               base=0, pattern=[[-1, P]], channel_multiplier=1).then_inc(ident_ready, 1)
            pool.wait_ge(ident_ready, 1)
            for n, s in enumerate(TURNED):
                if n:
                    pool.wait_ge(rows_zero, n)
                pool.memset(hist[P - BLOCK:P, s], 0.0).then_inc(rows_zero, 1)
            def one_round(rnd, slots, first, tail):
                for s in slots:
                    if (s == 2 * STEPS + 1 or (tail and s == TAIL - 1)) and not first:
                        wait(pool, out_copied, rnd, 1, 0)
                        pool.dma_start(out[bass.ds((rnd - 1) * ROUND, ROUND), :],
                                       out_sb[:, :]).then_inc(out_stored, 16)

            rounds(pool, one_round)

        @block.tensor
        def _(pe):
            pe.wait_ge(ident_ready, 1)
            pe.wait_ge(w_qk_loaded, 32)
            for n in range(2):
                mm = pe.transpose(ps_p[:, n * P:(n + 1) * P], w_in[:, n, :], ident[:, :])
            mm.then_inc(w_t_done, 1)
            pe.wait_ge(w_t_copied, 1)
            for h in range(H):
                rows = slice(h * HD, (h + 1) * HD)
                pe.matmul(ps_t[:, h, 0:P], w_t[rows, 0, :], w_t[rows, 1, :],
                          start=True, stop=True).then_inc(w_qk_done, 1)

            def one_round(rnd, slots, first, tail):
                for s in slots:
                    gr, k = divmod(s, STEPS)
                    def scores():
                        m = (s - LAG_S) % SLOTS
                        mg, mk = divmod(m, STEPS)
                        source = hist_t[mk % 2]
                        if not is_turned(first, s - LAG_S):
                            before = transposed_before(first, s - LAG_S)
                            wait(pe, low_copied, rnd, T_ROUND, before + 1)
                            wait(pe, high_copied, rnd, T_ROUND, before + 1)
                        else:
                            source = hist_x[MOVED_TO[TURNED.index(m)]]
                            before = turned_before(first, s - LAG_S)
                            wait(pe, x_moved_act, rnd, BY_ACT * X_ROUND, BY_ACT * (before + 1))
                            wait(pe, x_moved_dve, rnd, BY_DVE * X_ROUND, BY_DVE * (before + 1))
                        if mk == 0:
                            wait(pe, u_pad_ready, rnd, GROUPS, mg + 1)
                            wait(pe, scores_read, rnd, GROUPS, mg)
                        for g in range(TILES):
                            mm = pe.matmul(ps_s[32 * g:32 * g + 32, 0:PAIR * S], u_pad[mg % 2][:, mk, g, :],
                                           source[:, PAIR * g:PAIR * (g + 1), :],
                                           start=(mk == 0), stop=(mk == STEPS - 1))
                        mm.then_inc(scores_done, 1)

                    with_scores = not (first and s < LAG_S) and not (tail and s >= LAG_S)
                    if s == 0 and not tail:
                        wait(pe, x_loaded, rnd, 16, 16)
                        wait(pe, ctx_t_copied, rnd, PAIR * GROUPS, -2 * PAIR)
                        pe.transpose(ps_y[:, 0:ROUND], x_sb[:, :], ident[:, :]).then_inc(x_t_done, 1)
                    def probs_transpose(gp):
                        wait(pe, exp_done, rnd, GROUPS, gp)
                        if gp == 0 and not tail:
                            wait(pe, u_copied, rnd, 1, 1)
                        else:
                            wait(pe, p_pad_ready, rnd, 2 * GROUPS, 2 * (gp - 1))
                        for t in range(2):
                            mm = pe.transpose(ps_p[0:HALF, t * P:(t + 1) * P],
                                              probs[:, t * HALF:(t + 1) * HALF], ident[:, :])
                        mm.then_inc(probs_t_done, 1)

                    if not tail and not is_turned(first, s):
                        before = transposed_before(first, s)
                        wait(pe, hist_loaded[s], rnd, 32, 32)
                        for q in range(BANKS):
                            if first and s == 0:
                                pe.wait_ge(w_qk_act if q % 2 == 0 else w_qk_dve, 2)
                            if q == 0:
                                wait(pe, low_copied, rnd, T_ROUND, before)
                            if q == 2:
                                wait(pe, high_copied, rnd, T_ROUND, before)
                            for j in (2 * q, 2 * q + 1):
                                for t in range(2):
                                    at = (j % 2) * S + t * HALF
                                    mm = pe.transpose(ps_t[:, q, at:at + HALF], hist[0:HALF, s, j, t, :],
                                                      ident[0:HALF, 0:HALF])
                            if q == 1:
                                mm.then_inc(low_done, 1)
                            if q == 3:
                                mm.then_inc(high_done, 1)
                    if s == 0 and not tail:
                        wait(pe, x_t_copied, rnd, 1, 1)
                        wait(pe, p_pad_ready, rnd, 2 * GROUPS, -2)
                        for h in range(H):
                            mm = pe.matmul(ps_p[:, h * ROUND:(h + 1) * ROUND], w_qk[:, h, :],
                                           x_t[:, :], start=True, stop=True)
                        mm.then_inc(u_done, 1)
                    if first and s == STEPS:
                        pe.wait_ge(w_vo_loaded, 32)
                    if s == STEPS + 3 and not first:
                        wait(pe, ctx_t_copied, rnd, PAIR * GROUPS, 0)
                        for h in range(H):
                            mm = pe.matmul(ps_y[h * HD:(h + 1) * HD, 2 * P:3 * P],
                                           w_in[:, 2, h * HD:(h + 1) * HD], ctx_t[:, h, :],
                                           start=True, stop=True)
                        mm.then_inc(values_done, 1)
                    if s == STEPS + 4 and not first:
                        wait(pe, values_copied, rnd, 1, 0)
                        pe.matmul(ps_y[:, 3 * P:4 * P], values_t[:, :], w_in[:, 3, :],
                                  start=True, stop=True).then_inc(out_done, 1)
                    def context_transpose():
                        wait(pe, ctx_copied, rnd, GROUPS, gr - 1)
                        if gr == 0 and not tail:
                            wait(pe, x_t_copied, rnd, 1, 1)
                        elif gr == 2:
                            wait(pe, out_copied, rnd, 1, 0)
                        else:
                            wait(pe, ctx_t_copied, rnd, PAIR * GROUPS, PAIR * (gr - 2))
                        pe.transpose(ps_y[:, P:2 * P], ctx_sb[:, :], ident[:, :]).then_inc(ctx_t_done, 1)

                    def context_products(halves):
                        m = (s - LAG_C) % SLOTS
                        mg, mk = divmod(m, STEPS)
                        behind = GROUPS if s < LAG_C else 0
                        if mk == 0 and 0 in halves:
                            wait(pe, p_pad_ready, rnd, 2 * GROUPS, 2 * (mg + 1 - behind))
                            wait(pe, ctx_copied, rnd, GROUPS, mg - behind)
                        for t in halves:
                            for g in range(TILES):
                                mm = pe.matmul(ps_c[32 * g:32 * g + 32, :],
                                               p_pad[mg % 2][0:HALF, t, mk // 2, g, :],
                                               hist[0:HALF, m:m + 2, PAIR * g:PAIR * (g + 1), t, :],
                                               start=(mk == 0 and t == 0),
                                               stop=(mk == STEPS - 2 and t == 1))
                        if 1 in halves:
                            mm.then_inc(ctx_done, 1)

                    with_turn = k == 2 and not (first and gr < 2)
                    with_products = s % 2 == 0 and not (first and s < LAG_C) and not (tail and s >= LAG_C)
                    if with_turn and s in TURN_FIRST:
                        context_transpose()
                    if with_products and s in SPLIT_PRODUCTS:
                        context_products((0,))
                    if with_scores:
                        scores()
                    if k == 1 and not (first and gr == 0) and not (tail and gr > 0):
                        probs_transpose(gr)
                    if with_turn and s not in TURN_FIRST:
                        context_transpose()
                    if with_products:
                        context_products((1,) if s in SPLIT_PRODUCTS else (0, 1))

            rounds(pe, one_round)

        @block.scalar
        def _(act):
            act.wait_ge(w_t_done, 1)
            act.copy(w_t[:, :, :], ps_p[:, 0:2 * P].rearrange("p (n c) -> p n c", n=2)).then_inc(w_t_copied, 1)
            for h in (0, 2):
                act.wait_ge(w_qk_done, h + 1)
                act.mul(w_qk[:, h, :], ps_t[:, h, 0:P], -INV_SCALE).then_inc(w_qk_act, 1)

            def one_round(rnd, slots, first, tail):
                for s in slots:
                    gr, k = divmod(s, STEPS)
                    def move_blocks(start, stop):
                        for n, i in [] if tail else to_move(first, s)[start:stop]:
                            x = TURNED[n]
                            a, c = MOVE_ORDER[i]
                            wait(act, blocks_ready, rnd, PIECES * X_ROUND, PIECES * (turned_before(first, x) + 1))
                            wait(act, scores_done, rnd, SLOTS, moved_over(first, n))
                            act.copy(
                                moved(x, c, a, BLOCK), turned_block(x, a, c, BLOCK),
                            ).then_inc(x_moved_act, 1)

                    if s == 0 and not tail:
                        wait(act, x_t_done, rnd, 1, 1)
                        wait(act, u_done, rnd, 1, 0)
                        act.copy(x_t[:, :], ps_y[:, 0:ROUND]).then_inc(x_t_copied, 1)
                    move_blocks(0, MOVES_FIRST[s])
                    if not tail and not is_turned(first, s):
                        wait(act, low_done, rnd, T_ROUND, transposed_before(first, s) + 1)
                        wait(act, scores_done, rnd, SLOTS, s - 1)
                        act.copy(two_banks_to(hist_t[k % 2], 0), two_banks(0)).then_inc(low_copied, 1)
                    if s == 0 and not tail:
                        wait(act, u_done, rnd, 1, 1)
                        wait(act, u_pad_ready, rnd, GROUPS, 0)
                        act.copy(u_sb[:, :, :],
                                 ps_p[:, :].rearrange("p (h b) -> p b h", h=H)).then_inc(u_copied, 1)
                    if s == STEPS + 3 and not first:
                        wait(act, values_done, rnd, 1, 0)
                        act.copy(values_t[:, :], ps_y[:, 2 * P:3 * P]).then_inc(values_copied, 1)
                    move_blocks(MOVES_FIRST[s], BEFORE[s])
                    if k == 0 and not (first and gr == 0) and not (tail and gr > 0):
                        wait(act, max_ready, rnd, GROUPS, gr)
                        wait(act, probs_t_done, rnd, GROUPS, gr - 1)
                        wait(act, inv_ready, rnd, GROUPS, gr - 1)
                        act.activation(probs[:, :], neg_score[:, :], ACT.Exp, bias=neg_max[:, 0:1],
                                       scale=-1.0, accum_out=row_sum[:, 0:1]).then_inc(exp_done, 1)
                    if k == 2 and not (first and gr < 2):
                        g_of = (gr - 2) % GROUPS
                        wait(act, ctx_t_done, rnd, GROUPS, gr - 1)
                        if g_of == 0:
                            wait(act, values_done, rnd, 1, 0)
                        of_group = ctx_t[:, :, g_of * GROUP:(g_of + 1) * GROUP]
                        of_group = of_group.rearrange("p h (k g e) -> p e h g k", g=TILES, e=PAIR)
                        turned = ps_y[:, P:2 * P].rearrange("p (g k e h) -> p e h g k", g=TILES, e=PAIR, h=H)
                        for e in range(PAIR):
                            act.copy(of_group[:, e], turned[:, e]).then_inc(ctx_t_copied, 1)
                    move_blocks(BEFORE[s], MOVES[s])

            rounds(act, one_round)

        @block.vector
        def _(dve):
            for pad in p_pad:
                dve.memset(pad[:, :, :, :, :], 0.0).then_inc(p_pad_zero, 1)
            for pad in u_pad:
                dve.memset(pad[:, :, :, :], 0.0).then_inc(u_pad_zero, 1)
            dve.wait_ge(p_pad_zero, 2)
            dve.wait_ge(u_pad_zero, 2)
            dve.wait_ge(ident_ready, 1)
            dve.tensor_reduce(quad_sel[:, :], ident[:, :].rearrange("p (a c h) -> p c a h", c=QUAD, h=H),
                              mybir.AxisListType.XY, ALU.add).then_inc(sel_ready, 1)
            dve.tensor_reduce(pair_sel[:, :], ident[:, :].rearrange("p (a e h) -> p e a h", e=PAIR, h=H),
                              mybir.AxisListType.XY, ALU.add).then_inc(sel_ready, 1)
            dve.wait_ge(sel_ready, 2)
            for h in (1, 3):
                dve.wait_ge(w_qk_done, h + 1)
                dve.tensor_scalar(w_qk[:, h, :], ps_t[:, h, 0:P], -INV_SCALE, None, ALU.mult).then_inc(w_qk_dve, 1)

            def carry_waits(n):
                dve.tensor_copy(carrier[0:1, n:n + 1], pair_sel[0:1, 0:1])

            def turn_block(rnd, first, slot, n):
                if isinstance(rnd, int) and rnd == ROUNDS - 1 and slot >= SLOTS:
                    return
                over, s = divmod(slot, SLOTS)
                buffer = blocks[BLOCKS_IN[TURNED.index(s)]]
                read = turned_before(first, slot) - (2 if s == TURNED[0] else 1)
                wait(dve, x_moved_act, rnd, BY_ACT * X_ROUND, BY_ACT * read)
                wait(dve, x_moved_dve, rnd, BY_DVE * X_ROUND, BY_DVE * read)
                wait(dve, hist_loaded[s], rnd, 32, 32 * (over + 1))
                dve.transpose(
                    buffer[:, 4 * n:4 * n + 4, :].rearrange("p j d -> p (j d)"),
                    hist[:, s, 2 * n:2 * n + 2].rearrange("p j t d -> p (j t d)"),
                ).then_inc(blocks_ready, 1)

            def one_round(rnd, slots, first, tail):
                for s in slots:
                    gr, k = divmod(s, STEPS)
                    def copy_high():
                        wait(dve, high_done, rnd, T_ROUND, transposed_before(first, s) + 1)
                        wait(dve, scores_done, rnd, SLOTS, s - 1)
                        dve.tensor_copy(two_banks_to(hist_t[k % 2], 2), two_banks(2)).then_inc(high_copied, 1)

                    copies = not tail and not is_turned(first, s)
                    left_to_move = []
                    if not tail and s in DVE_MOVES and is_turned(first, DVE_MOVES[s]):
                        x = DVE_MOVES[s]
                        left_to_move = [(3, c, HALF - 3 * BLOCK) for c in range(4)]
                        left_to_move += [(a, c, BLOCK) for a, c in MOVE_ORDER[BY_ACT:]]

                    def move_next():
                        if left_to_move:
                            a, c, rows = left_to_move.pop(0)
                            wait(dve, blocks_ready, rnd, PIECES * X_ROUND, PIECES * (turned_before(first, x) + 1))
                            wait(dve, scores_done, rnd, SLOTS, moved_over(first, TURNED.index(x)))
                            dve.tensor_copy(moved(x, c, a, rows), turned_block(x, a, c, rows)).then_inc(x_moved_dve, 1)

                    def turn_share(start, stop):
                        for n, piece in [] if tail else to_turn(first, s)[start:stop]:
                            turn_block(rnd, first, (TURNED + (SLOTS + TURNED[0],))[n + 1], piece)

                    turn_share(0, TURNS_FIRST[s])
                    if copies and k != 1:
                        copy_high()
                    if not tail and (s == 0 or (k == 2 and gr < GROUPS - 1)):
                        ug = 0 if s == 0 else gr + 1
                        wait(dve, scores_done, rnd, SLOTS, STEPS * (ug - 1))
                        if s == 0:
                            wait(dve, u_copied, rnd, 1, 1)
                        dve.tensor_copy(
                            pad_columns(u_pad[ug % 2][:, :, :, :], STEPS, 8),
                            u_sb[:, ug * GROUP:(ug + 1) * GROUP, :].rearrange(
                                "p (k g e) h -> p k g (e h)", g=TILES, e=PAIR),
                        ).then_inc(u_pad_ready, 1)
                    if k == 0 and not (first and gr == 0) and not (tail and gr > 0):
                        wait(dve, scores_done, rnd, SLOTS, STEPS * gr)
                        wait(dve, filled, rnd, GROUPS, gr)
                        mask_in = mask_sb[(gr - 1) % GROUPS][:, :].rearrange("p (q t) -> p t q", t=2)
                        neg_halves = neg_score[:, :].rearrange("p (t q) -> p t q", t=2)
                        shares = ps_s[:, 0:2 * S].rearrange("p (e t q) -> p e t q", e=PAIR, t=2)
                        carry_waits(0)
                        dve.copy_predicated(neg_halves, mask_in, shares[:, 0]).then_inc(first_read, 1)
                        move_next()
                        wait(dve, mask_odd_ready, rnd, GROUPS, gr)
                        wait(dve, first_read, rnd, GROUPS, gr)
                        carry_waits(1)
                        dve.copy_predicated(neg_halves, mask_odd[:, :].rearrange("p (t q) -> p t q", t=2),
                                            shares[:, 1]).then_inc(scores_read, 1)
                        move_next()
                        wait(dve, scores_read, rnd, GROUPS, gr)
                        dve.tensor_reduce(neg_max[:, 0:1], neg_score[:, :], mybir.AxisListType.X,
                                          ALU.min).then_inc(max_ready, 1)
                    if k == 1 and not (first and gr < 2):
                        wait(dve, ctx_part_ready, rnd, GROUPS * (QUAD - 1), (QUAD - 1) * (gr - 2))
                        wait(dve, ctx_copied, rnd, GROUPS, gr - 2)
                        wait(dve, inv_ready, rnd, GROUPS, gr - 1)
                        dve.tensor_scalar(quad_inv[:, :], quad_sel[:, :], inv_sum[:, 0:1], None,
                                          ALU.mult).then_inc(quad_inv_ready, 1)
                        move_next()
                        wait(dve, quad_inv_ready, rnd, GROUPS, gr - 1)
                        wait(dve, ctx_done, rnd, SLOTS // 2, STEPS // 2 * (gr - 1))
                        dve.tensor_scalar(ctx_part[0][:, :], ps_c[:, 0:D], quad_inv[:, 0:1], None,
                                          ALU.mult).then_inc(ctx_part_ready, 1)
                        for c in range(1, QUAD):
                            last = c == QUAD - 1
                            move_next()
                            if copies and CTX_FIRST[gr] == c:
                                copy_high()
                            if last:
                                wait(dve, ctx_t_done, rnd, GROUPS, gr - 2)
                            wait(dve, ctx_part_ready, rnd, GROUPS * (QUAD - 1), (QUAD - 1) * (gr - 2) + c)
                            dve.scalar_tensor_tensor(
                                (ctx_sb if last else ctx_part[c])[:, :], ps_c[:, c * D:(c + 1) * D],
                                quad_inv[:, c:c + 1], ctx_part[c - 1][:, :], ALU.mult, ALU.add,
                            ).then_inc(ctx_copied if last else ctx_part_ready, 1)
                    if copies and k == 1 and (CTX_FIRST[gr] == QUAD or (first and gr < 2)):
                        copy_high()
                    if k == 1 and not (first and gr == 0) and not (tail and gr > 0):
                        par = (gr - 1) % 2
                        wait(dve, exp_done, rnd, GROUPS, gr)
                        wait(dve, quad_inv_ready, rnd, GROUPS, gr - 1)
                        dve.reciprocal(inv_sum[:, :], row_sum[:, :]).then_inc(inv_ready, 1)
                        wait(dve, ctx_done, rnd, SLOTS // 2, STEPS // 2 * (gr - 2))
                        wait(dve, probs_t_done, rnd, GROUPS, gr)
                        for t in range(2):
                            dve.tensor_copy(
                                pad_columns(p_pad[par][0:HALF, t], STEPS // 2, 16),
                                ps_p[0:HALF, t * P:(t + 1) * P].rearrange("p (g n c) -> p n g c", g=TILES, c=16),
                            ).then_inc(p_pad_ready, 1)
                    if k == 3 and not tail:
                        wait(dve, scores_read, rnd, GROUPS, gr)
                        wait(dve, mask_loaded[gr], rnd, 16, 16)
                        dve.tensor_scalar(mask_odd[:, :].rearrange("p (t q) -> p t q", t=2),
                                          mask_sb[gr][:, :].rearrange("p (q t) -> p t q", t=2),
                                          0.0, pair_sel[:, 1:2], ALU.not_equal, ALU.mult).then_inc(mask_odd_ready, 1)
                        wait(dve, exp_done, rnd, GROUPS, gr)
                        dve.memset(neg_score[:, :], NEG).then_inc(filled, 1)
                    while left_to_move:
                        move_next()
                    turn_share(TURNS_FIRST[s], None)
                    if s == SLOTS - 1 and not first:
                        wait(dve, out_stored, rnd, 16, 0)
                    if s == STEPS + 4 and not first:
                        wait(dve, out_done, rnd, 1, 0)
                        dve.tensor_copy(out_sb[:, :], ps_y[:, 3 * P:4 * P]).then_inc(out_copied, 1)

            rounds(dve, one_round, looks_ahead=True)


_INS = ["r_target_item", "r_history_sequence", "r_mask",
        "L0_rec_W_q", "L0_rec_W_k", "L0_rec_W_v", "L0_rec_W_o"]


def kernel(**inputs):
    import numpy as np
    import concourse.bacc as bacc
    from concourse.bass_utils import run_bass_kernel_spmd

    nc = bacc.Bacc("TRN2", target_bir_lowering=False, num_devices=1)
    arrays, args = {}, []
    for name in _INS:
        a = np.asarray(inputs[name])
        if name == "r_mask":
            a = a.reshape(-1, 4, 4, 2, a.shape[1]).transpose(0, 2, 1, 3, 4).reshape(a.shape)
        a = np.ascontiguousarray(a)
        arrays[name] = a
        args.append(nc.dram_tensor(name, a.shape, mybir.dt.from_np(a.dtype), kind="ExternalInput").ap())
    out = nc.dram_tensor("out", arrays["r_target_item"].shape, F32, kind="ExternalOutput").ap()
    target_attention(nc, *args, out)
    return run_bass_kernel_spmd(nc, [arrays], core_ids=[0]).results[0]["out"]
```
